# Optimizing a Trainium2 kernel written in Bass

```python
import numpy as np
import jax
import jax.numpy as jnp

def _softmax(x, axis=-1):
    return jax.nn.softmax(x, axis=axis)

def _gelu(x):
    return jax.nn.gelu(x, approximate=True)

def _silu(x):
    return jax.nn.silu(x)

def _sigmoid(x):
    return jax.nn.sigmoid(x)

def _layernorm(x, axis=-1, eps=1e-05):
    m = jnp.mean(x, axis=axis, keepdims=True)
    v = jnp.var(x, axis=axis, keepdims=True)
    return (x - m) / jnp.sqrt(v + eps)

def _scatter_add(tgt, idx, src, axis=0):
    return tgt.at[idx].add(src)

def _segment_sum(src, seg, n):
    return jax.ops.segment_sum(src, seg, n)
kernel_name = 'mk_adj_preln_d1_adj_r2_2ffb13'

def setup_inputs(seed: int=0):
    np.random.seed(seed)
    _w = jnp.asarray

    def _rec_inputs():
        import jax
        import jax.numpy as jnp
        _gk = jax.random.key(seed)
        x = -0.0001538 + 1 * jax.random.normal(jax.random.fold_in(_gk, 1), (64, 128, 384), jnp.float32)
        _a = jax.random.bernoulli(jax.random.fold_in(_gk, 2), 0.125, (64, 128, 128))
        _af = _a.astype(jnp.float32)
        _af = _af * jax.random.uniform(jax.random.fold_in(_gk, 3), (64, 128, 128), jnp.float32, 0.05, 0.999992)
        adj = _af
        return (x, adj)
    x, adj = _rec_inputs()

    def _L0_gnn_setup():
        import jax, jax.numpy as jnp
        import numpy as np
        B, N, D, H = (8, 512, 384, 12)
        HD = D // H

        def _split_heads(x):
            b, n, _ = x.shape
            return x.reshape(b, n, H, HD).transpose(0, 2, 1, 3)
        key = jax.random.key(seed)
        ks = jax.random.split(key, 10)
        input_graph = jax.random.normal(ks[0], (B, N, D), dtype=jnp.float32)
        u = jax.random.uniform(ks[1], (B, N, N), dtype=jnp.float32)
        keep = jax.random.uniform(ks[2], (B, N, N)) < 0.15
        adj = jnp.where(keep, u, 0.0)
        s = 1.0 / np.sqrt(D)
        Wq = jax.random.normal(ks[3], (D, D), dtype=jnp.float32) * s
        bq = jnp.zeros((D,), dtype=jnp.float32)
        Wk = jax.random.normal(ks[4], (D, D), dtype=jnp.float32) * s
        bk = jnp.zeros((D,), dtype=jnp.float32)
        Wv = jax.random.normal(ks[5], (D, D), dtype=jnp.float32) * s
        bv = jnp.zeros((D,), dtype=jnp.float32)
        beta = jnp.asarray(0.1, dtype=jnp.float32)
        return {'input_graph': input_graph, 'adj': adj, 'Wq': Wq, 'bq': bq, 'Wk': Wk, 'bk': bk, 'Wv': Wv, 'bv': bv, 'beta': beta}
    _L0_gnn_all = _L0_gnn_setup()
    _L0_gnn_in = {k: v for k, v in _L0_gnn_all.items() if k in ('Wq', 'bq', 'Wk', 'bk', 'Wv', 'bv', 'beta')}
    del _L0_gnn_all
    return {'x': x, 'adj': adj, 'L0_gnn_Wq': _L0_gnn_in['Wq'], 'L0_gnn_bq': _L0_gnn_in['bq'], 'L0_gnn_Wk': _L0_gnn_in['Wk'], 'L0_gnn_bk': _L0_gnn_in['bk'], 'L0_gnn_Wv': _L0_gnn_in['Wv'], 'L0_gnn_bv': _L0_gnn_in['bv'], 'L0_gnn_beta': _L0_gnn_in['beta']}

def reference(x, adj, L0_gnn_Wq, L0_gnn_bq, L0_gnn_Wk, L0_gnn_bk, L0_gnn_Wv, L0_gnn_bv, L0_gnn_beta):
    import jax
    import jax.numpy as jnp

    def _L0_gnn_ref(input_graph, adj, Wq, bq, Wk, bk, Wv, bv, beta):
        import jax, jax.numpy as jnp
        import numpy as np
        B, N, D, H = (8, 512, 384, 12)
        HD = D // H

        def _split_heads(x):
            b, n, _ = x.shape
            return x.reshape(b, n, H, HD).transpose(0, 2, 1, 3)
        q = _split_heads(input_graph @ Wq + bq)
        k = _split_heads(input_graph @ Wk + bk)
        v = _split_heads(input_graph @ Wv + bv)
        scores = jnp.einsum('bhqd,bhkd->bhqk', q, k) / jnp.sqrt(jnp.asarray(HD, input_graph.dtype))
        adj_e = adj[:, None, :, :]
        scores = scores + beta * adj_e
        scores = jnp.where(adj_e > 0, scores, jnp.asarray(-9000000000000000.0, scores.dtype))
        probs = jax.nn.softmax(scores, axis=-1)
        out = jnp.einsum('bhqk,bhkd->bhqd', probs, v)
        return out.transpose(0, 2, 1, 3).reshape(input_graph.shape[0], input_graph.shape[1], D)
    h = jnp.maximum(_layernorm(x, axis=-1), 0.0)
    x = x + _L0_gnn_ref(h, adj, L0_gnn_Wq, L0_gnn_bq, L0_gnn_Wk, L0_gnn_bk, L0_gnn_Wv, L0_gnn_bv, L0_gnn_beta)
    return x

_drawn_inputs = setup_inputs


def setup_inputs(seed=0):
    import zlib

    import numpy as np

    out = dict(_drawn_inputs(seed))
    spreads = {'L0_gnn_bq': (0.0, 0.8), 'L0_gnn_bk': (0.0, 0.8), 'L0_gnn_bv': (0.0, 0.1)}
    factors = {}
    for name, (base, spread) in spreads.items():
        noise = np.random.default_rng([zlib.crc32(name.encode()), seed]).standard_normal(out[name].shape)
        drawn = base * np.exp(spread * noise) if base else spread * noise
        out[name] = jnp.asarray(drawn.astype(out[name].dtype))
    for name, factor in factors.items():
        out[name] = (out[name] * factor).astype(out[name].dtype)
    return out
```

```python
from contextlib import ExitStack

import concourse.bass as bass
from concourse import mybir

F32 = mybir.dt.float32
F32R = mybir.dt.float32r
ALU = mybir.AluOpType
ACT = mybir.ActivationFunctionType
AX = mybir.AxisListType

HEADS = 12
GROUP = 4
EPS = 1e-5
MASKED = -9.0e15
RING = 4
QK_UNITS = 6
UNIT_A = [0, 2, 4, 5]
UNIT_B = [1, 3]


def gnn_attention(nc, x, adj, wq, bq, wk, bk, wv, bv, beta, out):
    B, N, D = x.shape
    HD = D // HEADS
    P = 128
    KC = D // P
    HC = P // HD
    NG = B // GROUP
    SCALE = float(HD) ** -0.5
    assert N == P and D % P == 0 and P % HD == 0 and KC == 3 and HC == 4 and NG == 16

    FIRST_LOOP, LAST_LOOP = 2, NG - 3

    x_v = x.rearrange("(g s) t d -> t g s d", s=GROUP)
    adj_v = adj.rearrange("(g s) q k -> q g s k", s=GROUP)

    with ExitStack() as ctx:
        def sb(name, shape, dt=F32):
            return ctx.enter_context(nc.sbuf_tensor(name, shape, dt))

        def pb(name, shape):
            return ctx.enter_context(nc.psum_tensor(name, shape, F32))

        def sem(name):
            return ctx.enter_context(nc.semaphore(name))

        w_raw = sb("w_raw", [P, KC, 3 * D])
        w_hi = sb("w_hi", [P, KC, 3 * D], F32R)
        w_lo = sb("w_lo", [P, KC, 3 * D], F32R)
        ident = sb("ident", [P, P])
        bq_raw = sb("bq_raw", [P, KC])
        bq_scaled = sb("bq_scaled", [P, KC])
        bk_col = sb("bk_col", [P, KC])
        bv_rows = sb("bv_rows", [P, D])
        beta_col = sb("beta_col", [P, 1])
        minus_half = sb("minus_half", [P, 1])
        eps_col = sb("eps_col", [P, 1])
        x_ring = sb("x_ring", [P, RING * GROUP * D])
        bn6 = sb("bn6", [P, 2, 6])
        meanvar = sb("meanvar", [P, 2, 2])
        var_eps = sb("var_eps", [P, 2])
        rstd = sb("rstd", [P, 2])
        xhat = sb("xhat", [P, 2, D])
        h_hi = [sb(f"h_hi{i}", [P, KC, GROUP * N], F32R) for i in range(2)]
        h_lo = [sb(f"h_lo{i}", [P, KC, GROUP * N], F32R) for i in range(2)]
        qk = [sb(f"qk{i}", [P, QK_UNITS, GROUP * N]) for i in range(2)]
        v = [sb(f"v{i}", [P, GROUP, D]) for i in range(2)]
        adj_in = [sb(f"adj_in{i}", [P, GROUP, N]) for i in range(2)]
        mask_term = sb("mask_term", [P, GROUP, N])
        bias = [sb(f"bias{i}", [P, GROUP, N]) for i in range(2)]
        probs = sb("probs", [P, 2, HC, KC, N])
        negmax = sb("negmax", [P, 2, HEADS])
        rowsum = sb("rowsum", [P, 2, HEADS])
        rinv = sb("rinv", [P, HEADS])
        probsT = sb("probsT", [P, KC, HC * N])
        outT = sb("outT", [P, D])
        y = sb("y", [P, 2, D])

        S_ps = pb("S_ps", [P, HC, 512])
        PT_ps = pb("PT_ps", [P, 2, 512])
        QK_ps = pb("QK_ps", [P, 512])
        G_ps = pb("G_ps", [P, 512])
        outT_ps = S_ps[:, 0, 0:D]
        out_ps = S_ps[:, 1, 0:D]

        w_loaded, const_loaded = sem("w_loaded"), sem("const_loaded")
        ident_zeroed, ident_ready = sem("ident_zeroed"), sem("ident_ready")
        consts_set = sem("consts_set")
        w_hi_ready, w_lo_ready = sem("w_hi_ready"), sem("w_lo_ready")
        bq_ready = sem("bq_ready")
        x_loaded = [sem(f"x_loaded{i}") for i in range(2)]
        adj_loaded = [sem(f"adj_loaded{i}") for i in range(2)]
        bn6_ready, stats_ready, eps_added, rstd_ready = sem("bn6_ready"), sem("stats_ready"), sem("eps_added"), sem("rstd_ready")
        xhat_ready, hT_in_psum = sem("xhat_ready"), sem("hT_in_psum")
        h_hi_stored, h_lo_stored = sem("h_hi_stored"), sem("h_lo_stored")
        v_in_psum, v_stored = sem("v_in_psum"), sem("v_stored")
        qk_in_psum, qk_stored = sem("qk_in_psum"), sem("qk_stored")
        mask_ready, bias_ready = sem("mask_ready"), sem("bias_ready")
        scores_in_psum, masked, negmax_ready = sem("scores_in_psum"), sem("masked"), sem("negmax_ready")
        probs_ready = [sem(f"probs_ready{m}") for m in range(KC)]
        pT_in_psum = [sem(f"pT_in_psum{m}") for m in range(KC)]
        pT_stored = [sem(f"pT_stored{m}") for m in range(KC)]
        pv_done = [sem(f"pv_done{m}") for m in range(KC)]
        outT_stored, out_in_psum = sem("outT_stored"), sem("out_in_psum")
        rinv_ready, normalised, y_ready = sem("rinv_ready"), sem("normalised"), sem("y_ready")
        out_written = [sem(f"out_written{i}") for i in range(2)]

        class Slot:

            def __init__(self, i, off, s):
                self.i, self.off, self.s = i, off, s
                self.static = isinstance(i, int)
                n = 2 * i + off if self.static else FIRST_LOOP
                self.T = -1 <= n <= NG - 2
                self.P = 0 <= n <= NG - 1
                self.A = 1 <= n <= NG
                self.O = 0 <= 4 * (n - 1) + s - 1 < B
                self.par = off % 2
                self.t = self.count(1)
                self.p = self.count(0)
                self.a = self.count(-1)
                self.o = self.a - 1
                if self.static and not self.T:
                    self.t = B
                if self.static and not self.P:
                    self.p = B if n >= NG else 0
                if self.static and n > NG:
                    self.a = B

            def count(self, d):
                return 8 * self.i + (4 * (self.off + d) + self.s)

            def groups(self, d):
                return 2 * self.i + (self.off + d)

            def pairs(self, d):
                return self.i + ((self.off + d) // 2 + 1)

            def units(self, u):
                return 12 * self.i + (QK_UNITS * self.off + u)

            def ring(self, d, s=0):
                half, low = (self.off + d) // 2, (self.off + d) % 2
                return ((self.i + half) % (RING // 2)) * (2 * GROUP * D) + (low * GROUP + s) * D

        def started(count):
            return not isinstance(count, int) or count > 0

        def slots(eng, body):
            for n in range(-1, FIRST_LOOP):
                for s in range(GROUP):
                    body(Slot(n // 2, n % 2, s))
            with eng.Fori(FIRST_LOOP // 2, (LAST_LOOP + 1) // 2) as i:
                for off in range(2):
                    for s in range(GROUP):
                        body(Slot(i, off, s))
            for n in range(LAST_LOOP + 1, NG + 1):
                for s in range(GROUP):
                    body(Slot(n // 2, n % 2, s))
            body(Slot((NG + 1) // 2, (NG + 1) % 2, 0))

        block = ctx.enter_context(nc.Block())

        @block.sync
        def _(sp):
            sp.dma_start(x_ring[:, 0:GROUP * D].rearrange("p (s d) -> p s d", s=GROUP), x_v[:, 0, :, :]).then_inc(x_loaded[0], 16)
            for c, w in enumerate((wq, wk, wv)):
                sp.dma_start(w_raw[:, :, c * D:(c + 1) * D], w.rearrange("(k p) n -> p k n", p=P)).then_inc(w_loaded, 16)
            with nc.allow_non_contiguous_dma(reason="bias columns, once"):
                sp.dma_start(bq_raw[:, :], bq.rearrange("(m p) -> p m", p=P)).then_inc(const_loaded, 16)
                sp.dma_start(bk_col[:, :], bk.rearrange("(m p) -> p m", p=P)).then_inc(const_loaded, 16)
            sp.dma_start(bv_rows[:, :], bv.rearrange("(a n) -> a n", a=1).broadcast_to([P, D])).then_inc(const_loaded, 16)
            sp.dma_start(beta_col[:, :], beta.rearrange("(a n) -> a n", a=1).broadcast_to([P, 1])).then_inc(const_loaded, 16)

            def slot(z):
                if z.O:
                    sp.wait_ge(y_ready, z.o + 1)
                    sp.dma_start(out[bass.ds(z.o, 1), :, :].rearrange("b t d -> t (b d)"),
                                 y[:, (z.s - 1) % 2, :]).then_inc(out_written[(z.s - 1) % 2], 16)
                if z.T and z.s == 0:
                    if started(z.groups(0)):
                        sp.wait_ge(bias_ready, z.groups(0))
                    sp.dma_start(adj_in[(z.par + 1) % 2][:, :, :],
                                 adj_v[:, bass.ds(z.groups(1), 1), :, :].rearrange("q g s k -> q (g s) k")).then_inc(adj_loaded[(z.par + 1) % 2], 16)
                    if not (z.static and z.groups(2) >= NG):
                        if started(z.count(-1)):
                            sp.wait_ge(y_ready, z.count(-1))
                        sp.dma_start(x_ring[:, bass.ds(z.ring(2), GROUP * D)].rearrange("p (s d) -> p s d", s=GROUP),
                                     x_v[:, bass.ds(z.groups(2), 1), :, :].rearrange("t g s d -> t (g s) d")).then_inc(x_loaded[z.par], 16)

            slots(sp, slot)
            for q in out_written:
                sp.wait_ge(q, 16 * B // 2)

        @block.gpsimd
        def _(pool):
            nc.gpsimd.memset(minus_half[:, :], -0.5).then_inc(consts_set, 1)
            nc.gpsimd.memset(eps_col[:, :], EPS).then_inc(consts_set, 1)
            nc.gpsimd.memset(ident[:, :], 0.0).then_inc(ident_zeroed, 1)
            pool.wait_ge(ident_zeroed, 1)
            nc.gpsimd.affine_select(out=ident[:, :], in_=ident[:, :], compare_op=ALU.not_equal, fill=1.0, base=0,
                                    pattern=[[-1, P]], channel_multiplier=1).then_inc(ident_ready, 1)
            pool.wait_ge(consts_set, 2)

            def slot(z):
                e = z.s % 2
                if z.T:
                    pool.wait_ge(stats_ready, z.t + 1)
                    nc.gpsimd.tensor_tensor(var_eps[:, e:e + 1], meanvar[:, e, 1:2], eps_col[:, :], ALU.add).then_inc(eps_added, 1)
                    pool.wait_ge(eps_added, z.t + 1)
                    if started(z.t - 1):
                        pool.wait_ge(xhat_ready, z.t - 1)
                    nc.gpsimd.tensor_tensor(rstd[:, e:e + 1], var_eps[:, e:e + 1], minus_half[:, :], ALU.pow).then_inc(rstd_ready, 1)
                if z.O:
                    e = (z.s - 1) % 2
                    xs = x_ring[:, bass.ds(z.ring(-1, z.s - 1) if z.s else z.ring(-2, GROUP - 1), D)]
                    pool.wait_ge(normalised, z.o + 1)
                    nc.gpsimd.tensor_tensor(y[:, e, :], y[:, e, :], xs, ALU.add).then_inc(y_ready, 1)

            slots(pool, slot)

        @block.scalar
        def _(act):
            act.wait_ge(w_loaded, 48)
            for c in range(3):
                nc.scalar.copy(w_hi[:, :, c * D:(c + 1) * D], w_raw[:, :, c * D:(c + 1) * D]).then_inc(w_hi_ready, 1)
            act.wait_ge(const_loaded, 64)
            nc.scalar.mul(bq_scaled[:, :], bq_raw[:, :], SCALE).then_inc(bq_ready, 1)
            act.wait_ge(bq_ready, 1)

            def store_probsT(z, m):
                act.wait_ge(pT_in_psum[m], z.o + 1)
                if started(z.o):
                    act.wait_ge(pv_done[m], z.o)
                nc.scalar.copy(probsT[:, m, :], PT_ps[:, m % 2, :]).then_inc(pT_stored[m], 1)

            def store_qk(z, u):
                act.wait_ge(qk_in_psum, z.units(u + 1))
                if started(z.count(-1) - z.s):
                    act.wait_ge(scores_in_psum, z.count(-1) - z.s)
                if u < KC:
                    nc.scalar.activation(qk[z.par][:, u, :], QK_ps[:, :], ACT.Identity, bias=bq_scaled[:, u:u + 1],
                                         scale=SCALE).then_inc(qk_stored, 1)
                else:
                    nc.scalar.activation(qk[z.par][:, u, :], QK_ps[:, :], ACT.Identity,
                                         bias=bk_col[:, u - KC:u - KC + 1]).then_inc(qk_stored, 1)

            def exponentials(z, m):
                e = z.s % 2
                if m == 0:
                    act.wait_ge(negmax_ready, z.a + 1)
                    if started(z.a - 1):
                        act.wait_ge(rinv_ready, z.a - 1)
                for j in range(HC):
                    s = probs[:, e, j, m, :]
                    last = nc.scalar.activation(s, s, ACT.Exp, bias=negmax[:, e, j * KC + m:j * KC + m + 1],
                                                accum_out=rowsum[:, e, m * HC + j:m * HC + j + 1])
                last.then_inc(probs_ready[m], 1)

            def slot(z):
                if z.O:
                    for m in range(KC):
                        store_probsT(z, m)
                if z.A:
                    exponentials(z, 0)
                if z.P:
                    store_qk(z, UNIT_A[z.s])
                if z.A:
                    exponentials(z, 1)
                if z.T:
                    act.wait_ge(hT_in_psum, z.t + 1)
                    nc.scalar.activation(h_hi[(z.par + 1) % 2][:, :, z.s * N:(z.s + 1) * N],
                                         G_ps[:, 0:D].rearrange("p (k t) -> p k t", k=KC), ACT.Relu).then_inc(h_hi_stored, 1)
                if z.A:
                    exponentials(z, 2)
                if z.P and z.s < 2:
                    store_qk(z, UNIT_B[z.s])

            slots(act, slot)

        @block.vector
        def _(dve):
            for c in range(3):
                dve.wait_ge(w_hi_ready, c + 1)
                ws = slice(c * D, (c + 1) * D)
                nc.vector.tensor_tensor(w_lo[:, :, ws], w_raw[:, :, ws], w_hi[:, :, ws].bitcast(F32), ALU.subtract).then_inc(w_lo_ready, 1)
            dve.wait_ge(const_loaded, 64)

            def slot(z):
                e, eo = z.s % 2, (z.s - 1) % 2
                if z.T:
                    xs = x_ring[:, bass.ds(z.ring(1, z.s), D)]
                    if z.s == 0:
                        dve.wait_ge(x_loaded[(z.par + 1) % 2], 16 * z.pairs(1))
                    nc.vector.bn_stats(bn6[:, e, :], xs).then_inc(bn6_ready, 1)
                    dve.wait_ge(bn6_ready, 1).then_inc(bn6_ready, -1)
                    nc.vector.bn_aggr(meanvar[:, e, :], bn6[:, e, :]).then_inc(stats_ready, 1)
                if z.A:
                    dve.wait_ge(scores_in_psum, z.a + 1)
                    if z.s == 0:
                        dve.wait_ge(bias_ready, z.groups(0))
                    if started(z.a - 1):
                        dve.wait_ge(pT_in_psum[2], z.a - 1)
                    nc.vector.tensor_tensor(probs[:, e, :, :, :], S_ps[:, :, 0:KC * N].rearrange("p j (m k) -> p j m k", m=KC),
                                            bias[(z.par + 1) % 2][:, z.s, :].unsqueeze(1).unsqueeze(1).broadcast_to([P, HC, KC, N]),
                                            ALU.add).then_inc(masked, 1)
                    dve.wait_ge(masked, z.a + 1)
                    nc.vector.tensor_reduce(negmax[:, e, :], probs[:, e, :, :, :].rearrange("p j m k -> p (j m) k"), axis=AX.X,
                                            op=ALU.max, negate=True).then_inc(negmax_ready, 1)
                if z.P:
                    dve.wait_ge(v_in_psum, z.p + 1)
                    if started(z.count(-2) + 1):
                        dve.wait_ge(pv_done[2], z.count(-2) + 1)
                    nc.vector.tensor_tensor(v[z.par][:, z.s, :], G_ps[:, 0:D], bv_rows[:, :], ALU.add).then_inc(v_stored, 1)
                if z.T:
                    dve.wait_ge(rstd_ready, z.t + 1)
                    if started(z.t - 1):
                        dve.wait_ge(hT_in_psum, z.t - 1)
                    nc.vector.tensor_scalar(xhat[:, e, :], xs, meanvar[:, e, 0:1], rstd[:, e:e + 1], ALU.subtract, ALU.mult).then_inc(xhat_ready, 1)
                if z.O:
                    dve.wait_ge(pv_done[2], z.o + 1)
                    if started(z.o):
                        dve.wait_ge(out_in_psum, z.o)
                    nc.vector.tensor_copy(outT[:, :], outT_ps).then_inc(outT_stored, 1)
                    dve.wait_ge(probs_ready[2], z.o + 1)
                    if started(z.o):
                        dve.wait_ge(normalised, z.o)
                    nc.vector.reciprocal(rinv[:, :], rowsum[:, eo, :]).then_inc(rinv_ready, 1)
                    dve.wait_ge(rinv_ready, z.o + 1)
                    dve.wait_ge(out_in_psum, z.o + 1)
                    if z.s == 0:
                        done = 4 * z.i + (2 * (z.off - 1) - 1)
                    else:
                        done = 4 * z.i + (2 * (z.off - 1) + (z.s - 1) // 2)
                    if started(done):
                        dve.wait_ge(out_written[eo], 16 * done)
                    nc.vector.tensor_tensor(y[:, eo, :].rearrange("p (h d) -> p h d", d=HD), out_ps.rearrange("p (h d) -> p h d", d=HD),
                                            rinv[:, :].unsqueeze(2).broadcast_to([P, HEADS, HD]), ALU.mult).then_inc(normalised, 1)
                if z.T:
                    hs = slice(z.s * N, (z.s + 1) * N)
                    dve.wait_ge(h_hi_stored, z.t + 1)
                    nc.vector.scalar_tensor_tensor(out=h_lo[(z.par + 1) % 2][:, :, hs], in0=G_ps[:, 0:D].rearrange("p (k t) -> p k t", k=KC),
                                                   scalar=0.0, in1=h_hi[(z.par + 1) % 2][:, :, hs].bitcast(F32),
                                                   op0=ALU.max, op1=ALU.subtract).then_inc(h_lo_stored, 1)
                if z.P and z.s == GROUP - 1:
                    dve.wait_ge(adj_loaded[z.par], 16 * z.pairs(0))
                    if started(z.groups(0)):
                        dve.wait_ge(bias_ready, z.groups(0))
                    nc.vector.tensor_scalar(mask_term[:, :, :], adj_in[z.par][:, :, :], 0.0, MASKED, ALU.is_le, ALU.mult).then_inc(mask_ready, 1)
                    dve.wait_ge(mask_ready, z.groups(1))
                    if started(z.count(-1) - z.s):
                        dve.wait_ge(masked, z.count(-1) - z.s)
                    nc.vector.scalar_tensor_tensor(out=bias[z.par][:, :, :], in0=adj_in[z.par][:, :, :], scalar=beta_col[:, 0:1],
                                                   in1=mask_term[:, :, :], op0=ALU.mult, op1=ALU.add).then_inc(bias_ready, 1)

            slots(dve, slot)

        @block.tensor
        def _(pe):
            pe.wait_ge(ident_ready, 1)

            def terms(z, k, cols, rows):
                hi, lo = h_hi[z.par], h_lo[z.par]
                return ((w_hi[:, k, cols], hi[:, k, rows]), (w_lo[:, k, cols], hi[:, k, rows]), (w_hi[:, k, cols], lo[:, k, rows]))

            def qk_matmuls(z, u, part):
                pairs = [t for k in range(KC) for t in terms(z, k, slice(u * P, (u + 1) * P), slice(0, GROUP * N))]
                if part[0] == 0:
                    if z.s == 0 and u == 0:
                        pe.wait_ge(h_lo_stored, z.count(1) if z.T else B)
                    if started(z.units(u)):
                        pe.wait_ge(qk_stored, z.units(u))
                for n in part:
                    last = nc.tensor.matmul(QK_ps[:, :], pairs[n][0], pairs[n][1], start=(n == 0), stop=(n == len(pairs) - 1))
                if part[-1] == len(pairs) - 1:
                    last.then_inc(qk_in_psum, 1)

            def transpose_probs(z, m):
                pe.wait_ge(probs_ready[m], z.o + 1)
                if m == 2:
                    pe.wait_ge(pT_stored[0], z.o + 1)
                elif started(z.o):
                    pe.wait_ge(pT_stored[2 - m], z.o)
                for j in range(HC):
                    last = nc.tensor.transpose(PT_ps[:, m % 2, j * N:(j + 1) * N], probs[:, (z.s - 1) % 2, j, m, :], ident[:, :])
                last.then_inc(pT_in_psum[m], 1)

            def probs_times_v(z, m):
                pe.wait_ge(pT_stored[m], z.o + 1)
                vo = v[(z.par + 1) % 2 if z.s else z.par]
                so = (z.s - 1) % GROUP
                for j in range(HC):
                    h = m * HC + j
                    last = nc.tensor.matmul(outT_ps[j * HD:(j + 1) * HD, m * N:(m + 1) * N], vo[:, so, h * HD:(h + 1) * HD],
                                            probsT[:, m, j * N:(j + 1) * N], start=True, stop=True, tile_position=(0, j * HD))
                last.then_inc(pv_done[m], 1)

            def slot(z):
                if z.A:
                    if z.s == 0:
                        pe.wait_ge(qk_stored, z.units(0))
                    if started(z.a):
                        pe.wait_ge(masked, z.a)
                    if started(z.a - 1):
                        pe.wait_ge(normalised, z.a - 1)
                    ts = slice(z.s * N, (z.s + 1) * N)
                    qk_a = qk[(z.par + 1) % 2]
                    for m in range(KC):
                        for j in range(HC):
                            rs = slice(j * HD, (j + 1) * HD)
                            last = nc.tensor.matmul(S_ps[:, j, m * N:(m + 1) * N], qk_a[rs, m, ts], qk_a[rs, KC + m, ts],
                                                    start=True, stop=True, tile_position=(j * HD, 0))
                    last.then_inc(scores_in_psum, 1)
                if z.O:
                    transpose_probs(z, 0)
                if z.P:
                    if not z.static or z.T or z.s == 0:
                        pe.wait_ge(h_lo_stored, z.t)
                    if z.static and z.s == 0 and z.p == 0:
                        pe.wait_ge(w_lo_ready, 3)
                    if started(z.p):
                        pe.wait_ge(v_stored, z.p)
                    pairs = [(hh, ww) for k in range(KC) for ww, hh in terms(z, k, slice(2 * D, 3 * D), slice(z.s * N, (z.s + 1) * N))]
                    for n, (hh, ww) in enumerate(pairs):
                        last = nc.tensor.matmul(G_ps[:, 0:D], hh, ww, start=(n == 0), stop=(n == len(pairs) - 1))
                    last.then_inc(v_in_psum, 1)
                if z.O:
                    transpose_probs(z, 1)
                    if z.A:
                        pe.wait_ge(masked, z.a + 1)
                    pe.wait_ge(v_stored, z.o + 1)
                    probs_times_v(z, 0)
                    transpose_probs(z, 2)
                    probs_times_v(z, 1)
                if z.P:
                    qk_matmuls(z, UNIT_A[z.s], range(0, 4))
                if z.O:
                    probs_times_v(z, 2)
                if z.P:
                    qk_matmuls(z, UNIT_A[z.s], range(4, 9))
                if z.O:
                    pe.wait_ge(outT_stored, z.o + 1)
                    for m in range(KC):
                        last = nc.tensor.transpose(out_ps[:, m * N:(m + 1) * N], outT[:, m * N:(m + 1) * N], ident[:, :])
                    last.then_inc(out_in_psum, 1)
                if z.T:
                    pe.wait_ge(xhat_ready, z.t + 1)
                    if z.P:
                        pe.wait_ge(v_stored, z.p + 1)
                    if started(z.t):
                        pe.wait_ge(h_lo_stored, z.t)
                    for k in range(KC):
                        last = nc.tensor.transpose(G_ps[:, k * N:(k + 1) * N], xhat[:, z.s % 2, k * P:(k + 1) * P], ident[:, :])
                    last.then_inc(hT_in_psum, 1)
                if z.P and z.s < 2:
                    qk_matmuls(z, UNIT_B[z.s], range(0, 9))

            slots(pe, slot)


_INS = ['x', 'adj', 'L0_gnn_Wq', 'L0_gnn_bq', 'L0_gnn_Wk', 'L0_gnn_bk', 'L0_gnn_Wv', 'L0_gnn_bv', 'L0_gnn_beta']


def kernel(**inputs):
    import numpy as _np
    import concourse.bacc as _bacc
    from concourse import mybir as _mybir
    from concourse.bass_utils import run_bass_kernel_spmd as _run

    nc = _bacc.Bacc("TRN2", target_bir_lowering=False, num_devices=1)
    arrays, args = {}, []
    for name in _INS:
        a = _np.ascontiguousarray(inputs[name])
        if a.ndim == 0:
            a = a.reshape(1)
        arrays[f"in_{name}_dram"] = a
        args.append(nc.dram_tensor(f"in_{name}_dram", a.shape, _mybir.dt.from_np(a.dtype), kind="ExternalInput").ap())
    out = nc.dram_tensor("out_0_dram", inputs["x"].shape, _mybir.dt.from_np(_np.dtype("float32")), kind="ExternalOutput").ap()
    gnn_attention(nc, *args, out)
    r = _run(nc, [arrays], core_ids=[0])
    return r.results[0]["out_0_dram"]
```

```python
from contextlib import ExitStack

import concourse.bass as bass
from concourse import mybir

F32 = mybir.dt.float32
F32R = mybir.dt.float32r
ALU = mybir.AluOpType
ACT = mybir.ActivationFunctionType
AX = mybir.AxisListType

HEADS = 12
GROUP = 4
EPS = 1e-5
MASKED = -9.0e15
RING = 4
QK_UNITS = 6
UNIT_A = [0, 2, 4, 5]
UNIT_B = [1, 3]


def gnn_attention(nc, x, adj, wq, bq, wk, bk, wv, bv, beta, out):
    B, N, D = x.shape
    HD = D // HEADS
    P = 128
    KC = D // P
    HC = P // HD
    NG = B // GROUP
    SCALE = float(HD) ** -0.5
    assert N == P and D % P == 0 and P % HD == 0 and KC == 3 and HC == 4 and NG == 16

    FIRST_LOOP, LAST_LOOP = 2, NG - 3

    x_v = x.rearrange("(g s) t d -> t g s d", s=GROUP)
    adj_v = adj.rearrange("(g s) q k -> q g s k", s=GROUP)

    with ExitStack() as ctx:
        def sb(name, shape, dt=F32):
            return ctx.enter_context(nc.sbuf_tensor(name, shape, dt))

        def pb(name, shape):
            return ctx.enter_context(nc.psum_tensor(name, shape, F32))

        def sem(name):
            return ctx.enter_context(nc.semaphore(name))

        w_raw = sb("w_raw", [P, KC, 3 * D])
        w_hi = sb("w_hi", [P, KC, 3 * D], F32R)
        w_lo = sb("w_lo", [P, KC, 3 * D], F32R)
        ident = sb("ident", [P, P])
        bq_raw = sb("bq_raw", [P, KC])
        bq_scaled = sb("bq_scaled", [P, KC])
        bk_col = sb("bk_col", [P, KC])
        bv_rows = sb("bv_rows", [P, D])
        beta_col = sb("beta_col", [P, 1])
        minus_half = sb("minus_half", [P, 1])
        eps_col = sb("eps_col", [P, 1])
        x_ring = sb("x_ring", [P, RING * GROUP * D])
        bn6 = sb("bn6", [P, GROUP, 6])
        meanvar = sb("meanvar", [P, GROUP, 2])
        var_eps = sb("var_eps", [P, GROUP])
        rstd = sb("rstd", [P, GROUP])
        xhat = sb("xhat", [P, GROUP, D])
        h_hi = [sb(f"h_hi{i}", [P, KC, GROUP * N], F32R) for i in range(2)]
        h_lo = [sb(f"h_lo{i}", [P, KC, GROUP * N], F32R) for i in range(2)]
        qk = [sb(f"qk{i}", [P, QK_UNITS, GROUP * N]) for i in range(2)]
        adj_in = [sb(f"adj_in{i}", [P, GROUP, N]) for i in range(2)]
        mask_term = sb("mask_term", [P, GROUP, N])
        bias = [sb(f"bias{i}", [P, GROUP, N]) for i in range(2)]
        probs = sb("probs", [P, 2, HC, KC, N])
        v = sb("v", [P, 2, D])
        negmax = sb("negmax", [P, 2, HEADS])
        rowsum = sb("rowsum", [P, 2, HEADS])
        rinv = sb("rinv", [P, HEADS])
        probsT = sb("probsT", [P, KC, HC * N])
        outT = sb("outT", [P, D])
        y = sb("y", [P, 2, D])

        S_ps = pb("S_ps", [P, HC, 512])
        PT_ps = pb("PT_ps", [P, 2, 512])
        G_ps = pb("G_ps", [P, 2, 512])
        outT_ps = S_ps[:, 0, 0:D]
        out_ps = PT_ps[:, 1, 0:D]

        w_loaded, const_loaded = [sem(f"w_loaded{c}") for c in range(3)], sem("const_loaded")
        ident_zeroed, ident_ready = sem("ident_zeroed"), sem("ident_ready")
        consts_set = sem("consts_set")
        w_hi_ready, w_lo_ready = sem("w_hi_ready"), sem("w_lo_ready")
        bq_ready = sem("bq_ready")
        x_loaded = [sem(f"x_loaded{i}") for i in range(2)]
        adj_loaded = [sem(f"adj_loaded{i}") for i in range(2)]
        bn6_ready, stats_ready, eps_added, rstd_ready = sem("bn6_ready"), sem("stats_ready"), sem("eps_added"), sem("rstd_ready")
        xhat_ready, hT_in_psum = sem("xhat_ready"), sem("hT_in_psum")
        h_hi_stored, h_lo_stored = sem("h_hi_stored"), sem("h_lo_stored")
        qk_in_psum, qk_stored = sem("qk_in_psum"), sem("qk_stored")
        mask_ready, bias_ready = sem("mask_ready"), sem("bias_ready")
        v_in_psum, v_stored = sem("v_in_psum"), sem("v_stored")
        scores_in_psum, masked, negmax_ready = sem("scores_in_psum"), sem("masked"), sem("negmax_ready")
        probs_ready = [sem(f"probs_ready{m}") for m in range(KC)]
        pT_in_psum = [sem(f"pT_in_psum{m}") for m in range(KC)]
        pT_stored = [sem(f"pT_stored{m}") for m in range(KC)]
        pv_done = [sem(f"pv_done{m}") for m in range(KC)]
        outT_stored, out_in_psum = sem("outT_stored"), sem("out_in_psum")
        rinv_ready, normalised, y_ready = sem("rinv_ready"), sem("normalised"), sem("y_ready")
        out_written = [sem(f"out_written{i}") for i in range(2)]

        class Slot:

            def __init__(self, i, off, s):
                self.i, self.off, self.s = i, off, s
                self.static = isinstance(i, int)
                n = 2 * i + off if self.static else FIRST_LOOP
                self.T = -1 <= n <= NG - 2
                self.P = 0 <= n <= NG - 1
                self.A = 1 <= n <= NG
                self.O = 0 <= 4 * (n - 1) + s - 1 < B
                self.par = off % 2
                self.t = self.count(1)
                self.a = self.count(-1)
                self.o = self.a - 1
                if self.static and not self.T:
                    self.t = B
                if self.static and n > NG:
                    self.a = B

            def count(self, d):
                return 8 * self.i + (4 * (self.off + d) + self.s)

            def groups(self, d):
                return 2 * self.i + (self.off + d)

            def pairs(self, d):
                return self.i + ((self.off + d) // 2 + 1)

            def units(self, u):
                return 12 * self.i + (QK_UNITS * self.off + u)

            def ring(self, d, s=0):
                half, low = (self.off + d) // 2, (self.off + d) % 2
                return ((self.i + half) % (RING // 2)) * (2 * GROUP * D) + (low * GROUP + s) * D

        def hT_bank(z):
            if z.static and not z.A:
                return S_ps[:, z.s, 0:D]
            return G_ps[:, 0 if z.s < 2 else 1, 0:D]

        def started(count):
            return not isinstance(count, int) or count > 0

        def slots(eng, body):
            for n in range(-1, FIRST_LOOP):
                for s in range(GROUP):
                    body(Slot(n // 2, n % 2, s))
            with eng.Fori(FIRST_LOOP // 2, (LAST_LOOP + 1) // 2) as i:
                for off in range(2):
                    for s in range(GROUP):
                        body(Slot(i, off, s))
            for n in range(LAST_LOOP + 1, NG + 1):
                for s in range(GROUP):
                    body(Slot(n // 2, n % 2, s))
            body(Slot((NG + 1) // 2, (NG + 1) % 2, 0))

        block = ctx.enter_context(nc.Block())

        @block.sync
        def _(sp):
            sp.dma_start(x_ring[:, 0:GROUP * D].rearrange("p (s d) -> p s d", s=GROUP), x_v[:, 0, :, :]).then_inc(x_loaded[0], 16)
            for c, w in enumerate((wq, wk, wv)):
                sp.dma_start(w_raw[:, :, c * D:(c + 1) * D], w.rearrange("(k p) n -> p k n", p=P)).then_inc(w_loaded[c], 16)
            with nc.allow_non_contiguous_dma(reason="bias columns, once"):
                sp.dma_start(bq_raw[:, :], bq.rearrange("(m p) -> p m", p=P)).then_inc(const_loaded, 16)
                sp.dma_start(bk_col[:, :], bk.rearrange("(m p) -> p m", p=P)).then_inc(const_loaded, 16)
            sp.dma_start(bv_rows[:, :], bv.rearrange("(a n) -> a n", a=1).broadcast_to([P, D])).then_inc(const_loaded, 16)
            sp.dma_start(beta_col[:, :], beta.rearrange("(a n) -> a n", a=1).broadcast_to([P, 1])).then_inc(const_loaded, 16)

            def slot(z):
                if z.O:
                    sp.wait_ge(y_ready, z.o + 1)
                    sp.dma_start(out[bass.ds(z.o, 1), :, :].rearrange("b t d -> t (b d)"),
                                 y[:, (z.s - 1) % 2, :]).then_inc(out_written[(z.s - 1) % 2], 16)
                if z.T and z.s == 0:
                    if started(z.groups(0)):
                        sp.wait_ge(bias_ready, z.groups(0))
                    sp.dma_start(adj_in[(z.par + 1) % 2][:, :, :],
                                 adj_v[:, bass.ds(z.groups(1), 1), :, :].rearrange("q g s k -> q (g s) k")).then_inc(adj_loaded[(z.par + 1) % 2], 16)
                    if not (z.static and z.groups(2) >= NG):
                        if started(z.t):
                            sp.wait_ge(stats_ready, z.t)
                        if started(z.count(-1)):
                            sp.wait_ge(y_ready, z.count(-1))
                        sp.dma_start(x_ring[:, bass.ds(z.ring(2), GROUP * D)].rearrange("p (s d) -> p s d", s=GROUP),
                                     x_v[:, bass.ds(z.groups(2), 1), :, :].rearrange("t g s d -> t (g s) d")).then_inc(x_loaded[z.par], 16)

            slots(sp, slot)
            for q in out_written:
                sp.wait_ge(q, 16 * B // 2)

        @block.gpsimd
        def _(pool):
            nc.gpsimd.memset(minus_half[:, :], -0.5).then_inc(consts_set, 1)
            nc.gpsimd.memset(eps_col[:, :], EPS).then_inc(consts_set, 1)
            nc.gpsimd.memset(ident[:, :], 0.0).then_inc(ident_zeroed, 1)
            pool.wait_ge(ident_zeroed, 1)
            nc.gpsimd.affine_select(out=ident[:, :], in_=ident[:, :], compare_op=ALU.not_equal, fill=1.0, base=0,
                                    pattern=[[-1, P]], channel_multiplier=1).then_inc(ident_ready, 1)
            pool.wait_ge(consts_set, 2)

            def slot(z):
                e = z.s
                if z.T:
                    pool.wait_ge(stats_ready, z.t + 1)
                    nc.gpsimd.tensor_tensor(var_eps[:, e:e + 1], meanvar[:, e, 1:2], eps_col[:, :], ALU.add).then_inc(eps_added, 1)
                    pool.wait_ge(eps_added, z.t + 1)
                    if started(z.t - 3):
                        pool.wait_ge(xhat_ready, z.t - 3)
                    nc.gpsimd.tensor_tensor(rstd[:, e:e + 1], var_eps[:, e:e + 1], minus_half[:, :], ALU.pow).then_inc(rstd_ready, 1)
                if z.O:
                    e = (z.s - 1) % 2
                    xs = x_ring[:, bass.ds(z.ring(-1, z.s - 1) if z.s else z.ring(-2, GROUP - 1), D)]
                    pool.wait_ge(normalised, z.o + 1)
                    nc.gpsimd.tensor_tensor(y[:, e, :], y[:, e, :], xs, ALU.add).then_inc(y_ready, 1)

            slots(pool, slot)

        @block.scalar
        def _(act):
            def weights_high(c):
                act.wait_ge(w_loaded[c], 16)
                nc.scalar.copy(w_hi[:, :, c * D:(c + 1) * D], w_raw[:, :, c * D:(c + 1) * D]).then_inc(w_hi_ready, 1)

            weights_high(0)
            weights_high(1)

            def store_probsT(z, m):
                act.wait_ge(pT_in_psum[m], z.o + 1)
                if started(z.o):
                    act.wait_ge(pv_done[m], z.o)
                nc.scalar.copy(probsT[:, m, :], PT_ps[:, m % 2, :]).then_inc(pT_stored[m], 1)

            def store_qk(z, u):
                bank = G_ps[:, 0 if u in UNIT_A else 1, :]
                act.wait_ge(qk_in_psum, z.units(u + 1))
                if started(z.count(-1) - z.s):
                    act.wait_ge(scores_in_psum, z.count(-1) - z.s)
                if u < KC:
                    nc.scalar.activation(qk[z.par][:, u, :], bank, ACT.Identity, bias=bq_scaled[:, u:u + 1],
                                         scale=SCALE).then_inc(qk_stored, 1)
                else:
                    nc.scalar.activation(qk[z.par][:, u, :], bank, ACT.Identity,
                                         bias=bk_col[:, u - KC:u - KC + 1]).then_inc(qk_stored, 1)

            def exponentials(z, m):
                e = z.s % 2
                if m == 0:
                    act.wait_ge(negmax_ready, z.a + 1)
                    if started(z.a - 1):
                        act.wait_ge(rinv_ready, z.a - 1)
                for j in range(HC):
                    s = probs[:, e, j, m, :]
                    last = nc.scalar.activation(s, s, ACT.Exp, bias=negmax[:, e, j * KC + m:j * KC + m + 1],
                                                accum_out=rowsum[:, e, m * HC + j:m * HC + j + 1])
                last.then_inc(probs_ready[m], 1)

            def high_part(z):
                act.wait_ge(hT_in_psum, z.t + 1)
                nc.scalar.activation(h_hi[(z.par + 1) % 2][:, :, z.s * N:(z.s + 1) * N],
                                     hT_bank(z).rearrange("p (k t) -> p k t", k=KC), ACT.Relu).then_inc(h_hi_stored, 1)

            def slot(z):
                if z.T and not z.A and not z.P:
                    high_part(z)
                if z.O:
                    for m in range(KC):
                        store_probsT(z, m)
                if z.A:
                    exponentials(z, 0)
                if z.P:
                    store_qk(z, UNIT_A[z.s])
                if z.T and (z.s >= 2 if z.A else z.P):
                    high_part(z)
                if z.A:
                    exponentials(z, 1)
                    exponentials(z, 2)
                if z.P and z.s < 2:
                    store_qk(z, UNIT_B[z.s])
                if z.T and z.A and z.s < 2:
                    high_part(z)
                if z.static and z.T and not z.P and z.s == GROUP - 1:
                    weights_high(2)
                    act.wait_ge(const_loaded, 64)
                    nc.scalar.mul(bq_scaled[:, :], bq_raw[:, :], SCALE).then_inc(bq_ready, 1)
                    act.wait_ge(bq_ready, 1)

            slots(act, slot)

        @block.vector
        def _(dve):
            def weights_low(c):
                dve.wait_ge(w_hi_ready, c + 1)
                ws = slice(c * D, (c + 1) * D)
                nc.vector.tensor_tensor(w_lo[:, :, ws], w_raw[:, :, ws], w_hi[:, :, ws].bitcast(F32), ALU.subtract).then_inc(w_lo_ready, 1)

            def statistics(z):
                if z.s == 0:
                    dve.wait_ge(x_loaded[(z.par + 1) % 2], 16 * z.pairs(1))
                nc.vector.bn_stats(bn6[:, z.s, :], x_ring[:, bass.ds(z.ring(1, z.s), D)]).then_inc(bn6_ready, 1)
                dve.wait_ge(bn6_ready, 1).then_inc(bn6_ready, -1)
                nc.vector.bn_aggr(meanvar[:, z.s, :], bn6[:, z.s, :]).then_inc(stats_ready, 1)

            def normalise(z):
                dve.wait_ge(rstd_ready, z.t + 1)
                if started(z.t - 3):
                    dve.wait_ge(hT_in_psum, z.t - 3)
                nc.vector.tensor_scalar(xhat[:, z.s, :], x_ring[:, bass.ds(z.ring(1, z.s), D)], meanvar[:, z.s, 0:1],
                                        rstd[:, z.s:z.s + 1], ALU.subtract, ALU.mult).then_inc(xhat_ready, 1)

            def low_part(z):
                hs = slice(z.s * N, (z.s + 1) * N)
                dve.wait_ge(h_hi_stored, z.t + 1)
                nc.vector.scalar_tensor_tensor(out=h_lo[(z.par + 1) % 2][:, :, hs], in0=hT_bank(z).rearrange("p (k t) -> p k t", k=KC),
                                               scalar=0.0, in1=h_hi[(z.par + 1) % 2][:, :, hs].bitcast(F32),
                                               op0=ALU.max, op1=ALU.subtract).then_inc(h_lo_stored, 1)

            def values(z):
                dve.wait_ge(v_in_psum, z.a + 1)
                if started(z.a - 1):
                    dve.wait_ge(pv_done[2], z.a - 1)
                nc.vector.tensor_tensor(v[:, z.s % 2, :], G_ps[:, 1, 0:D], bv_rows[:, :], ALU.add).then_inc(v_stored, 1)

            def slot(z):
                e, eo = z.s % 2, (z.s - 1) % 2
                ahead = z.static and z.T and not z.A
                first = ahead and not z.P
                if ahead and z.s == 0:
                    group = [Slot(z.i, z.off, s) for s in range(GROUP)]
                    for w in group:
                        statistics(w)
                    for w in group:
                        normalise(w)
                    if first:
                        weights_low(0)
                if z.A:
                    dve.wait_ge(scores_in_psum, z.a + 1)
                    if z.s == 0:
                        dve.wait_ge(bias_ready, z.groups(0))
                    if started(z.a - 1):
                        dve.wait_ge(pT_in_psum[2], z.a - 1)
                    nc.vector.tensor_tensor(probs[:, e, :, :, :], S_ps[:, :, 0:KC * N].rearrange("p j (m k) -> p j m k", m=KC),
                                            bias[(z.par + 1) % 2][:, z.s, :].unsqueeze(1).unsqueeze(1).broadcast_to([P, HC, KC, N]),
                                            ALU.add).then_inc(masked, 1)
                    dve.wait_ge(masked, z.a + 1)
                    nc.vector.tensor_reduce(negmax[:, e, :], probs[:, e, :, :, :].rearrange("p j m k -> p (j m) k"), axis=AX.X,
                                            op=ALU.max, negate=True).then_inc(negmax_ready, 1)
                if z.A and (z.P or not z.O):
                    values(z)
                if z.T and z.A:
                    statistics(z)
                if z.T and z.A and not z.O:
                    normalise(z)
                if z.O:
                    dve.wait_ge(pv_done[2], z.o + 1)
                    if started(z.o):
                        dve.wait_ge(out_in_psum, z.o)
                    nc.vector.tensor_copy(outT[:, :], outT_ps).then_inc(outT_stored, 1)
                    if z.A and not z.P:
                        values(z)
                    dve.wait_ge(probs_ready[2], z.o + 1)
                    if started(z.o):
                        dve.wait_ge(normalised, z.o)
                    nc.vector.reciprocal(rinv[:, :], rowsum[:, eo, :]).then_inc(rinv_ready, 1)
                    if z.T:
                        normalise(z)
                    dve.wait_ge(rinv_ready, z.o + 1)
                    dve.wait_ge(out_in_psum, z.o + 1)
                    if z.s == 0:
                        done = 4 * z.i + (2 * (z.off - 1) - 1)
                    else:
                        done = 4 * z.i + (2 * (z.off - 1) + (z.s - 1) // 2)
                    if started(done):
                        dve.wait_ge(out_written[eo], 16 * done)
                    nc.vector.tensor_tensor(y[:, eo, :].rearrange("p (h d) -> p h d", d=HD), out_ps.rearrange("p (h d) -> p h d", d=HD),
                                            rinv[:, :].unsqueeze(2).broadcast_to([P, HEADS, HD]), ALU.mult).then_inc(normalised, 1)
                if z.T:
                    low_part(z)
                if first and z.s == GROUP - 1:
                    weights_low(1)
                    weights_low(2)
                    dve.wait_ge(const_loaded, 64)
                if z.P and z.s == GROUP - 1:
                    dve.wait_ge(adj_loaded[z.par], 16 * z.pairs(0))
                    if started(z.groups(0)):
                        dve.wait_ge(bias_ready, z.groups(0))
                    nc.vector.tensor_scalar(mask_term[:, :, :], adj_in[z.par][:, :, :], 0.0, MASKED, ALU.is_le, ALU.mult).then_inc(mask_ready, 1)
                    dve.wait_ge(mask_ready, z.groups(1))
                    if started(z.count(-1) - z.s):
                        dve.wait_ge(masked, z.count(-1) - z.s)
                    nc.vector.scalar_tensor_tensor(out=bias[z.par][:, :, :], in0=adj_in[z.par][:, :, :], scalar=beta_col[:, 0:1],
                                                   in1=mask_term[:, :, :], op0=ALU.mult, op1=ALU.add).then_inc(bias_ready, 1)

            slots(dve, slot)

        @block.tensor
        def _(pe):
            pe.wait_ge(ident_ready, 1)

            def terms(par, k, cols, rows):
                hi, lo = h_hi[par], h_lo[par]
                return ((w_hi[:, k, cols], hi[:, k, rows]), (w_lo[:, k, cols], hi[:, k, rows]), (w_hi[:, k, cols], lo[:, k, rows]))

            def qk_matmuls(z, u, part):
                pairs = [t for k in range(KC) for t in terms(z.par, k, slice(u * P, (u + 1) * P), slice(0, GROUP * N))]
                bank = 0 if u in UNIT_A else 1
                if part[0] == 0:
                    if z.static and z.units(u) in (0, KC):
                        pe.wait_ge(w_lo_ready, 1 + u // KC)
                    if bank == 1:
                        if z.A:
                            pe.wait_ge(v_stored, z.a + 1)
                        elif started(z.units(u - 1)):
                            pe.wait_ge(qk_stored, z.units(u - 1))
                    else:
                        if z.s == 0 or (z.T and z.A):
                            pe.wait_ge(h_lo_stored, z.t)
                        before = z.units(u - (u - 1 in UNIT_B))
                        if started(before):
                            pe.wait_ge(qk_stored, before)
                for n in part:
                    last = nc.tensor.matmul(G_ps[:, bank, :], pairs[n][0], pairs[n][1], start=(n == 0), stop=(n == len(pairs) - 1))
                if part[-1] == len(pairs) - 1:
                    last.then_inc(qk_in_psum, 1)

            def transpose_probs(z, m):
                pe.wait_ge(probs_ready[m], z.o + 1)
                if m == 2:
                    pe.wait_ge(pT_stored[0], z.o + 1)
                elif m == 1 and started(z.o):
                    pe.wait_ge(normalised, z.o)
                elif started(z.o):
                    pe.wait_ge(pT_stored[2], z.o)
                for j in range(HC):
                    last = nc.tensor.transpose(PT_ps[:, m % 2, j * N:(j + 1) * N], probs[:, (z.s - 1) % 2, j, m, :], ident[:, :])
                last.then_inc(pT_in_psum[m], 1)

            def probs_times_v(z, m):
                pe.wait_ge(pT_stored[m], z.o + 1)
                for j in range(HC):
                    h = m * HC + j
                    last = nc.tensor.matmul(outT_ps[j * HD:(j + 1) * HD, m * N:(m + 1) * N], v[:, (z.s - 1) % 2, h * HD:(h + 1) * HD],
                                            probsT[:, m, j * N:(j + 1) * N], start=True, stop=True, tile_position=(0, j * HD))
                last.then_inc(pv_done[m], 1)

            def transpose_xhat(z):
                pe.wait_ge(xhat_ready, z.t + 1)
                bank_used = z.t - GROUP + 1 if z.static and not z.A else z.t
                if started(bank_used):
                    pe.wait_ge(h_lo_stored, bank_used)
                if not z.A:
                    pass
                elif z.P and z.s < 2:
                    pe.wait_ge(qk_stored, z.units(UNIT_A[z.s] + 1))
                elif z.s >= 2:
                    pe.wait_ge(v_stored, z.a + 1)
                for k in range(KC):
                    last = nc.tensor.transpose(hT_bank(z)[:, k * N:(k + 1) * N], xhat[:, z.s, k * P:(k + 1) * P], ident[:, :])
                last.then_inc(hT_in_psum, 1)

            def values(z, part):
                if part[0] == 0:
                    if z.T or z.s == 0:
                        pe.wait_ge(h_lo_stored, z.t)
                    if z.s == 0 or z.P:
                        pe.wait_ge(qk_stored, z.units(UNIT_A[z.s]) if z.P else QK_UNITS * NG)
                    if z.static and z.a == 0:
                        pe.wait_ge(w_lo_ready, 3)
                    if started(z.a):
                        pe.wait_ge(v_stored, z.a)
                pairs = [(hh, ww) for k in range(KC)
                         for ww, hh in terms((z.par + 1) % 2, k, slice(2 * D, 3 * D), slice(z.s * N, (z.s + 1) * N))]
                for n in part:
                    last = nc.tensor.matmul(G_ps[:, 1, 0:D], pairs[n][0], pairs[n][1], start=(n == 0), stop=(n == len(pairs) - 1))
                if part[-1] == len(pairs) - 1:
                    last.then_inc(v_in_psum, 1)

            def slot(z):
                if z.T and not z.A and not z.P:
                    transpose_xhat(z)
                if z.A:
                    if z.s == 0:
                        pe.wait_ge(qk_stored, z.units(-1))
                    if z.static and z.a == 0:
                        pe.wait_ge(h_lo_stored, z.t)
                    if started(z.a):
                        pe.wait_ge(masked, z.a)
                    if started(z.a - 1):
                        pe.wait_ge(outT_stored, z.a - 1)
                    ts = slice(z.s * N, (z.s + 1) * N)
                    qk_a = qk[(z.par + 1) % 2]
                    for m in range(KC):
                        if z.s == 0 and m == KC - 1:
                            pe.wait_ge(qk_stored, z.units(0))
                        for j in range(HC):
                            rs = slice(j * HD, (j + 1) * HD)
                            last = nc.tensor.matmul(S_ps[:, j, m * N:(m + 1) * N], qk_a[rs, m, ts], qk_a[rs, KC + m, ts],
                                                    start=True, stop=True, tile_position=(j * HD, 0))
                    last.then_inc(scores_in_psum, 1)
                if z.O:
                    transpose_probs(z, 0)
                split = 9 if z.P or not z.O else 6
                if z.A:
                    values(z, range(0, split))
                if z.O:
                    transpose_probs(z, 1)
                    if z.A:
                        pe.wait_ge(masked, z.a + 1)
                    pe.wait_ge(v_stored, z.o + 1)
                    probs_times_v(z, 0)
                    transpose_probs(z, 2)
                    probs_times_v(z, 1)
                if z.P:
                    qk_matmuls(z, UNIT_A[z.s], range(0, 4))
                if z.O:
                    probs_times_v(z, 2)
                if z.P:
                    qk_matmuls(z, UNIT_A[z.s], range(4, 9))
                if z.T and z.P and not z.A:
                    transpose_xhat(z)
                if z.A and split < 9:
                    values(z, range(split, 9))
                if z.O:
                    pe.wait_ge(outT_stored, z.o + 1)
                    pe.wait_ge(pT_stored[1], z.o + 1)
                    for m in range(KC):
                        last = nc.tensor.transpose(out_ps[:, m * N:(m + 1) * N], outT[:, m * N:(m + 1) * N], ident[:, :])
                    last.then_inc(out_in_psum, 1)
                if z.P and z.s < 2:
                    qk_matmuls(z, UNIT_B[z.s], range(0, 9))
                if z.T and z.A:
                    transpose_xhat(z)

            slots(pe, slot)


_INS = ['x', 'adj', 'L0_gnn_Wq', 'L0_gnn_bq', 'L0_gnn_Wk', 'L0_gnn_bk', 'L0_gnn_Wv', 'L0_gnn_bv', 'L0_gnn_beta']


def kernel(**inputs):
    import numpy as _np
    import concourse.bacc as _bacc
    from concourse import mybir as _mybir
    from concourse.bass_utils import run_bass_kernel_spmd as _run

    nc = _bacc.Bacc("TRN2", target_bir_lowering=False, num_devices=1)
    arrays, args = {}, []
    for name in _INS:
        a = _np.ascontiguousarray(inputs[name])
        if a.ndim == 0:
            a = a.reshape(1)
        arrays[f"in_{name}_dram"] = a
        args.append(nc.dram_tensor(f"in_{name}_dram", a.shape, _mybir.dt.from_np(a.dtype), kind="ExternalInput").ap())
    out = nc.dram_tensor("out_0_dram", inputs["x"].shape, _mybir.dt.from_np(_np.dtype("float32")), kind="ExternalOutput").ap()
    gnn_attention(nc, *args, out)
    r = _run(nc, [arrays], core_ids=[0])
    return r.results[0]["out_0_dram"]
```
